# Optimizing a Trainium2 kernel written in Bass

```python
import numpy as np
import jax
import jax.numpy as jnp

def _softmax(x, axis=-1):
    return jax.nn.softmax(x, axis=axis)

def _gelu(x):
    return jax.nn.gelu(x, approximate=True)

def _silu(x):
    return jax.nn.silu(x)

def _sigmoid(x):
    return jax.nn.sigmoid(x)

def _layernorm(x, axis=-1, eps=1e-05):
    m = jnp.mean(x, axis=axis, keepdims=True)
    v = jnp.var(x, axis=axis, keepdims=True)
    return (x - m) / jnp.sqrt(v + eps)

def _scatter_add(tgt, idx, src, axis=0):
    return tgt.at[idx].add(src)

def _segment_sum(src, seg, n):
    return jax.ops.segment_sum(src, seg, n)
kernel_name = 'mk_dlrm_tower_d1_rec_r8_db43e5'

def setup_inputs(seed: int=0):
    np.random.seed(seed)
    _w = jnp.asarray

    def _rec_inputs():
        import jax
        import jax.numpy as jnp
        _tk = jax.random.key(seed)
        ids = jnp.stack([jax.random.randint(jax.random.fold_in(_tk, 200 + f), (512,), 0, v, jnp.int32) for f, v in enumerate([1000, 1250, 1250, 12500, 1000, 1250, 12500, 1000, 125000, 1250, 1250, 1000, 1000, 1000, 1250, 1000, 12500, 1000, 12500, 12500, 1250, 1250, 12500, 1000, 1250, 12500])], axis=1)
        tbl_0 = 0.05 * jax.random.normal(jax.random.fold_in(_tk, 500 + 0), (1000, 128), jnp.float32)
        tbl_1 = 0.05 * jax.random.normal(jax.random.fold_in(_tk, 500 + 1), (1250, 128), jnp.float32)
        tbl_2 = 0.05 * jax.random.normal(jax.random.fold_in(_tk, 500 + 2), (1250, 128), jnp.float32)
        tbl_3 = 0.05 * jax.random.normal(jax.random.fold_in(_tk, 500 + 3), (12500, 128), jnp.float32)
        tbl_4 = 0.05 * jax.random.normal(jax.random.fold_in(_tk, 500 + 4), (1000, 128), jnp.float32)
        tbl_5 = 0.05 * jax.random.normal(jax.random.fold_in(_tk, 500 + 5), (1250, 128), jnp.float32)
        tbl_6 = 0.05 * jax.random.normal(jax.random.fold_in(_tk, 500 + 6), (12500, 128), jnp.float32)
        tbl_7 = 0.05 * jax.random.normal(jax.random.fold_in(_tk, 500 + 7), (1000, 128), jnp.float32)
        tbl_8 = 0.05 * jax.random.normal(jax.random.fold_in(_tk, 500 + 8), (125000, 128), jnp.float32)
        tbl_9 = 0.05 * jax.random.normal(jax.random.fold_in(_tk, 500 + 9), (1250, 128), jnp.float32)
        tbl_10 = 0.05 * jax.random.normal(jax.random.fold_in(_tk, 500 + 10), (1250, 128), jnp.float32)
        tbl_11 = 0.05 * jax.random.normal(jax.random.fold_in(_tk, 500 + 11), (1000, 128), jnp.float32)
        tbl_12 = 0.05 * jax.random.normal(jax.random.fold_in(_tk, 500 + 12), (1000, 128), jnp.float32)
        tbl_13 = 0.05 * jax.random.normal(jax.random.fold_in(_tk, 500 + 13), (1000, 128), jnp.float32)
        tbl_14 = 0.05 * jax.random.normal(jax.random.fold_in(_tk, 500 + 14), (1250, 128), jnp.float32)
        tbl_15 = 0.05 * jax.random.normal(jax.random.fold_in(_tk, 500 + 15), (1000, 128), jnp.float32)
        tbl_16 = 0.05 * jax.random.normal(jax.random.fold_in(_tk, 500 + 16), (12500, 128), jnp.float32)
        tbl_17 = 0.05 * jax.random.normal(jax.random.fold_in(_tk, 500 + 17), (1000, 128), jnp.float32)
        tbl_18 = 0.05 * jax.random.normal(jax.random.fold_in(_tk, 500 + 18), (12500, 128), jnp.float32)
        tbl_19 = 0.05 * jax.random.normal(jax.random.fold_in(_tk, 500 + 19), (12500, 128), jnp.float32)
        tbl_20 = 0.05 * jax.random.normal(jax.random.fold_in(_tk, 500 + 20), (1250, 128), jnp.float32)
        tbl_21 = 0.05 * jax.random.normal(jax.random.fold_in(_tk, 500 + 21), (1250, 128), jnp.float32)
        tbl_22 = 0.05 * jax.random.normal(jax.random.fold_in(_tk, 500 + 22), (12500, 128), jnp.float32)
        tbl_23 = 0.05 * jax.random.normal(jax.random.fold_in(_tk, 500 + 23), (1000, 128), jnp.float32)
        tbl_24 = 0.05 * jax.random.normal(jax.random.fold_in(_tk, 500 + 24), (1250, 128), jnp.float32)
        tbl_25 = 0.05 * jax.random.normal(jax.random.fold_in(_tk, 500 + 25), (12500, 128), jnp.float32)
        _rk = jax.random.fold_in(_tk, 7)
        r_dense_x = -0.000514642 + 1.00011 * jax.random.normal(jax.random.fold_in(_rk, 101), (512, 128), jnp.float32)
        W_top1 = 0.0456912 * jax.random.normal(jax.random.fold_in(_tk, 801), (479, 512), jnp.float32)
        W_top2 = 0.0441942 * jax.random.normal(jax.random.fold_in(_tk, 802), (512, 256), jnp.float32)
        W_top3 = 0.0625 * jax.random.normal(jax.random.fold_in(_tk, 803), (256, 1), jnp.float32)
        b_top1 = jnp.zeros((512,), jnp.float32)
        b_top2 = jnp.zeros((256,), jnp.float32)
        return (r_dense_x, ids, tbl_0, tbl_1, tbl_2, tbl_3, tbl_4, tbl_5, tbl_6, tbl_7, tbl_8, tbl_9, tbl_10, tbl_11, tbl_12, tbl_13, tbl_14, tbl_15, tbl_16, tbl_17, tbl_18, tbl_19, tbl_20, tbl_21, tbl_22, tbl_23, tbl_24, tbl_25, W_top1, b_top1, W_top2, b_top2, W_top3)
    r_dense_x, ids, tbl_0, tbl_1, tbl_2, tbl_3, tbl_4, tbl_5, tbl_6, tbl_7, tbl_8, tbl_9, tbl_10, tbl_11, tbl_12, tbl_13, tbl_14, tbl_15, tbl_16, tbl_17, tbl_18, tbl_19, tbl_20, tbl_21, tbl_22, tbl_23, tbl_24, tbl_25, W_top1, b_top1, W_top2, b_top2, W_top3 = _rec_inputs()

    def _L0_rec_setup():
        import jax, jax.numpy as jnp
        import numpy as np
        F = 26
        D = 128
        B = 2048
        _TRIU_I, _TRIU_J = np.triu_indices(F + 1, k=1)
        _TRIU_I = jnp.asarray(_TRIU_I)
        _TRIU_J = jnp.asarray(_TRIU_J)
        key = jax.random.key(seed)
        k1, k2 = jax.random.split(key)
        sparse_x = jax.random.normal(k1, (B, F, D), dtype=jnp.float32)
        dense_x = jax.random.normal(k2, (B, D), dtype=jnp.float32)
        return {'sparse_x': sparse_x, 'dense_x': dense_x}
    _L0_rec_all = _L0_rec_setup()
    _L0_rec_in = {k: v for k, v in _L0_rec_all.items() if k in ()}
    del _L0_rec_all
    return {'r_dense_x': r_dense_x, 'ids': ids, 'tbl_0': tbl_0, 'tbl_1': tbl_1, 'tbl_2': tbl_2, 'tbl_3': tbl_3, 'tbl_4': tbl_4, 'tbl_5': tbl_5, 'tbl_6': tbl_6, 'tbl_7': tbl_7, 'tbl_8': tbl_8, 'tbl_9': tbl_9, 'tbl_10': tbl_10, 'tbl_11': tbl_11, 'tbl_12': tbl_12, 'tbl_13': tbl_13, 'tbl_14': tbl_14, 'tbl_15': tbl_15, 'tbl_16': tbl_16, 'tbl_17': tbl_17, 'tbl_18': tbl_18, 'tbl_19': tbl_19, 'tbl_20': tbl_20, 'tbl_21': tbl_21, 'tbl_22': tbl_22, 'tbl_23': tbl_23, 'tbl_24': tbl_24, 'tbl_25': tbl_25, 'W_top1': W_top1, 'b_top1': b_top1, 'W_top2': W_top2, 'b_top2': b_top2, 'W_top3': W_top3}

def reference(r_dense_x, ids, tbl_0, tbl_1, tbl_2, tbl_3, tbl_4, tbl_5, tbl_6, tbl_7, tbl_8, tbl_9, tbl_10, tbl_11, tbl_12, tbl_13, tbl_14, tbl_15, tbl_16, tbl_17, tbl_18, tbl_19, tbl_20, tbl_21, tbl_22, tbl_23, tbl_24, tbl_25, W_top1, b_top1, W_top2, b_top2, W_top3):
    import jax
    import jax.numpy as jnp

    def _L0_rec_ref(sparse_x, dense_x):
        import jax, jax.numpy as jnp
        import numpy as np
        F = 26
        D = 128
        B = 2048
        _TRIU_I, _TRIU_J = np.triu_indices(F + 1, k=1)
        _TRIU_I = jnp.asarray(_TRIU_I)
        _TRIU_J = jnp.asarray(_TRIU_J)
        combined = jnp.concatenate([sparse_x, dense_x[:, None, :]], axis=1)
        interact = jnp.einsum('bfd,bgd->bfg', combined, combined)
        return interact[:, _TRIU_I, _TRIU_J]
    e = jnp.stack([tbl_0[ids[:, 0]], tbl_1[ids[:, 1]], tbl_2[ids[:, 2]], tbl_3[ids[:, 3]], tbl_4[ids[:, 4]], tbl_5[ids[:, 5]], tbl_6[ids[:, 6]], tbl_7[ids[:, 7]], tbl_8[ids[:, 8]], tbl_9[ids[:, 9]], tbl_10[ids[:, 10]], tbl_11[ids[:, 11]], tbl_12[ids[:, 12]], tbl_13[ids[:, 13]], tbl_14[ids[:, 14]], tbl_15[ids[:, 15]], tbl_16[ids[:, 16]], tbl_17[ids[:, 17]], tbl_18[ids[:, 18]], tbl_19[ids[:, 19]], tbl_20[ids[:, 20]], tbl_21[ids[:, 21]], tbl_22[ids[:, 22]], tbl_23[ids[:, 23]], tbl_24[ids[:, 24]], tbl_25[ids[:, 25]]], axis=1)
    z = _L0_rec_ref(e, r_dense_x)
    z = z.reshape(z.shape[0], -1)
    h = jnp.concatenate([z, r_dense_x], axis=1)
    h = jnp.maximum(h @ W_top1 + b_top1, 0.0)
    h = jnp.maximum(h @ W_top2 + b_top2, 0.0)
    y = h @ W_top3
    return y

_drawn_inputs = setup_inputs


def setup_inputs(seed=0):
    import zlib

    import numpy as np

    out = dict(_drawn_inputs(seed))
    spreads = {'b_top1': (0.0, 0.1), 'b_top2': (0.0, 0.1)}
    factors = {}
    for name, (base, spread) in spreads.items():
        noise = np.random.default_rng([zlib.crc32(name.encode()), seed]).standard_normal(out[name].shape)
        drawn = base * np.exp(spread * noise) if base else spread * noise
        out[name] = jnp.asarray(drawn.astype(out[name].dtype))
    for name, factor in factors.items():
        out[name] = (out[name] * factor).astype(out[name].dtype)
    return out
```

```python
from contextlib import ExitStack

import numpy as np

import concourse.bass as bass
from concourse import mybir

P = 128
B = 512
D = 128
N_FIELDS = 26
N_SLOTS = 27
N1, N2 = 512, 256
TILES = B // P
Q = 4
G = P // Q
PAD = 32

ONEHOT = [0, 4, 7, 11, 12, 13]
OH_CHUNKS = 8
OH_K = 1000 // OH_CHUNKS
GATHERED = [f for f in range(N_FIELDS) if f not in ONEHOT]
NG = len(GATHERED)
NO = len(ONEHOT)
SLOT_FIELD = [N_FIELDS] + GATHERED + ONEHOT
NT = -(-(NG + 1) // 4)
NJ = N_SLOTS - 1
SETS = 4
SET_G = G // SETS
RECTS = [(1, 2)] + [(j, 3) for j in range(3, N_SLOTS, 3)]
NC = 3


def rect_at(r):
    return sum(nj * (j0 + nj - 1) for j0, nj in RECTS[:r])


N_PACKED = rect_at(len(RECTS))
assert N_PACKED <= NC * P
ACT_RECTS = [8, 7]

ALU = mybir.AluOpType
ACT = mybir.ActivationFunctionType
F32 = mybir.dt.float32
F16 = mybir.dt.float16
BF16 = mybir.dt.bfloat16
I32 = mybir.dt.int32


def tower(nc, dense, ids, ids_by_field, tables, w1_pairs, w1_dense, b1, w2, b2, w3, out):
    with ExitStack() as ctx:
        def sb(name, shape, dt=F32):
            return ctx.enter_context(nc.sbuf_tensor(name, shape, dt))

        def psum(name, shape):
            return ctx.enter_context(nc.psum_tensor(name, shape, F32))

        def sem(name):
            return ctx.enter_context(nc.semaphore(name))

        ids_sb = sb("ids_sb", [P, TILES, N_FIELDS], I32)
        dense_sb = sb("dense_sb", [P, TILES, D])
        rows = sb("rows", [P, TILES, NG, D])
        xt = sb("xt", [P, TILES, P, PAD])
        dense_t = sb("dense_t", [P, TILES, P])
        gram_sb = sb("gram_sb", [P, NJ, G])
        pairs = sb("pairs", [P, NJ, PAD])
        packed = sb("packed", [P, NC * P])
        pairs_t = sb("pairs_t", [P, NC, P])
        h1 = sb("h1", [P, N1 // P, P])
        h2 = sb("h2", [P, N2 // P, P])
        y_sb = sb("y_sb", [P, TILES])
        w1p_sb = sb("w1p_sb", [P, NC, N1])
        w1d_sb = sb("w1d_sb", [P, N1])
        w2_sb = sb("w2_sb", [P, N1 // P, N2])
        w3_sb = sb("w3_sb", [P, N2 // P])
        b1_sb = sb("b1_sb", [P, N1 // P])
        b2_sb = sb("b2_sb", [P, N2 // P])
        ident = sb("ident", [P, P])
        row_of = sb("row_of", [P, OH_CHUNKS], I32)
        row_f = sb("row_f", [P, OH_CHUNKS])
        id_rows = sb("id_rows", [P, NO, B], I32)
        id16 = sb("id16", [P, 2, B], F16)
        onehot = sb("onehot", [P, 2, OH_CHUNKS, B], BF16)
        table = sb("table", [P, 3, OH_CHUNKS, D])
        rest = sb("rest", [P, 2, OH_CHUNKS, D])
        low = sb("low", [P, 2, OH_CHUNKS, D], BF16)

        tr_ps = [psum(f"tr_ps{i}", [P, 4, P]) for i in range(2)]
        gram_ps = [psum(f"gram_ps{i}", [P, 2, 512]) for i in range(2)]
        act_ps = psum("act_ps", [P, 512])
        dve_ps = psum("dve_ps", [P, 512])
        pick_ps = [act_ps, dve_ps]

        ids_in = sem("ids_in")
        dense_in = sem("dense_in")
        weights_in = sem("weights_in")
        id_rows_in = sem("id_rows_in")
        table_in = [sem(f"table_in{i}") for i in range(3)]
        gathered = [[sem(f"gathered{t}_{n}") for n in range(NT)] for t in range(TILES)]
        ident_zero = sem("ident_zero")
        consts = sem("consts")
        row_ready = sem("row_ready")
        pad_zero = sem("pad_zero")
        id16_ready = sem("id16_ready")
        rest_ready = sem("rest_ready")
        picks_ready = sem("picks_ready")
        pick_done = sem("pick_done")
        pick_out = sem("pick_out")
        tr_ready = sem("tr_ready")
        tr_out_dve = sem("tr_out_dve")
        tr_out_act = sem("tr_out_act")
        gram_ready = sem("gram_ready")
        gram_out_dve = sem("gram_out_dve")
        gram_out_act = sem("gram_out_act")
        pairs_ready = sem("pairs_ready")
        packed_dve = sem("packed_dve")
        packed_act = sem("packed_act")
        back_ready = sem("back_ready")
        back_out_dve = sem("back_out_dve")
        back_out_act = sem("back_out_act")
        h1_ready = sem("h1_ready")
        h1_out_dve = sem("h1_out_dve")
        h1_out_act = sem("h1_out_act")
        h2_ready = sem("h2_ready")
        h2_out_dve = sem("h2_out_dve")
        h2_out_act = sem("h2_out_act")
        y_ready = sem("y_ready")
        y_out = sem("y_out")
        stored = sem("stored")

        block = ctx.enter_context(nc.Block())

        def bank_slots(n):
            return range(4 * n, min(4 * n + 4, NG + 1))

        def gram_block(s, q):
            return gram_sb[PAD * q:PAD * (q + 1), :, s * SET_G:(s + 1) * SET_G].rearrange("i j (b g) -> i j b g", b=2)

        def gram_block_ps(s, q):
            v = gram_ps[s % 2][PAD * q:PAD * (q + 1), :, 0:4 * Q * NJ].rearrange("i b (g n) -> i b g n", g=4)
            return v[:, :, :, q * NJ:(q + 1) * NJ].rearrange("i b g j -> i j b g")

        def high_half(ap):
            v = ap.bitcast(BF16)
            return v.rearrange("p c (d h) -> p c d h", h=2)[:, :, :, 1]

        def group_order(bank, w):
            return bank[:, 0:w, :].rearrange("d s (q g) -> d g q s", q=Q)

        def tile_slots(t, n):
            w = len(bank_slots(n))
            return xt[:, t, :, 4 * n:4 * n + w].rearrange("d (g q) s -> d g q s", q=Q)

        def rect(r):
            j0, nj = RECTS[r]
            ni = j0 + nj - 1
            to = packed[:, rect_at(r):rect_at(r) + nj * ni].rearrange("p (j i) -> p j i", j=nj)
            return to, pairs[:, j0 - 1:j0 - 1 + nj, 0:ni]

        @block.sync
        def _(sp):
            sp.dma_start(ids_sb[:], ids.rearrange("(p t) f -> p t f", t=TILES)).then_inc(ids_in, 16)
            for o in range(NO):
                if o == 0:
                    sp.dma_start(id_rows[0:OH_K], ids_by_field.rearrange("(a o) b -> a o b", a=1)
                                 .to_broadcast([OH_K, NO, B])).then_inc(id_rows_in, 16)
                if o >= 3:
                    sp.wait_ge(pick_done, o - 2)
                sp.dma_start(table[0:OH_K, o % 3], tables[ONEHOT[o]].rearrange("(p c) d -> p c d", c=OH_CHUNKS)
                             ).then_inc(table_in[o % 3], 16)
                if o == 0:
                    sp.dma_start(dense_sb[:], dense.rearrange("(p t) d -> p t d", t=TILES)).then_inc(dense_in, 16)
            sp.wait_ge(y_out, TILES)
            sp.dma_start(out.rearrange("(p t) o -> p (t o)", t=TILES), y_sb[:]).then_inc(stored, 16)
            sp.wait_ge(stored, 16)

        @block.gpsimd
        def _(pool):
            pool.memset(ident[:], 0.0).then_inc(ident_zero, 1)
            pool.iota(row_of[:], pattern=[[1, OH_CHUNKS]], base=0, channel_multiplier=OH_CHUNKS).then_inc(row_ready, 1)
            pool.wait_ge(ident_zero, 1)
            pool.affine_select(out=ident[:], in_=ident[:], compare_op=ALU.not_equal, fill=1.0, base=0,
                               pattern=[[-1, P]], channel_multiplier=1).then_inc(consts, 1)
            pool.wait_ge(ids_in, 16)
            for t in range(TILES):
                for s in range(1, NG + 1):
                    f = SLOT_FIELD[s]
                    pool.indirect_dma_start(rows[:, t, s - 1, :], None, tables[f],
                                            bass.IndirectOffsetOnAxis(ids_sb[:, t, f:f + 1], 0)
                                            ).then_inc(gathered[t][s // 4], 16)

        @block.scalar
        def _(act):
            act.dma_start(w1p_sb[:], w1_pairs).then_inc(weights_in, 16)
            act.dma_start(w1d_sb[:], w1_dense).then_inc(weights_in, 16)
            act.dma_start(w2_sb[:], w2.rearrange("(c k) n -> k c n", k=P)).then_inc(weights_in, 16)
            act.dma_start(w3_sb[:], w3).then_inc(weights_in, 16)
            act.dma_start(b1_sb[:], b1).then_inc(weights_in, 16)
            act.dma_start(b2_sb[:], b2).then_inc(weights_in, 16)
            for o in range(NO):
                act.wait_ge(pick_done, o + 1)
                act.activation(xt[:, :, :, NG + 1 + o], pick_ps[o % 2][:].rearrange("d (t p) -> d t p", t=TILES),
                               ACT.Copy).then_inc(pick_out, 1)
            act.wait_ge(weights_in, 96)
            with act.Fori(0, TILES) as t:
                for n in range(1, NT, 2):
                    w = len(bank_slots(n))
                    act.wait_ge(tr_ready, t * NT + (n + 1))
                    act.activation(tile_slots(t, n), group_order(tr_ps[1], w), ACT.Copy).then_inc(tr_out_act, 1)
                act.wait_ge(pairs_ready, t + 1)
                for s in range(SETS):
                    act.wait_ge(gram_ready, t * SETS + (s + 1))
                    for q in (0, 1):
                        last = act.activation(gram_block(s, q), gram_block_ps(s, q), ACT.Copy)
                    last.then_inc(gram_out_act, 1)
                act.wait_ge(pairs_ready, t + 2)
                for r in ACT_RECTS:
                    last = act.activation(*rect(r), ACT.Copy)
                last.then_inc(packed_act, 1)
                act.wait_ge(back_ready, t + 1)
                act.activation(pairs_t[:, 0, :], act_ps[:, 0:P], ACT.Copy).then_inc(back_out_act, 1)
                act.wait_ge(h1_ready, t + 1)
                for m in (0, 1):
                    last = act.activation(h1[:, m, :], act_ps[:, m * P:(m + 1) * P], ACT.Relu, bias=b1_sb[:, m:m + 1])
                last.then_inc(h1_out_act, 1)
                act.wait_ge(h2_ready, t + 1)
                act.activation(h2[:, 0, :], act_ps[:, 0:P], ACT.Relu, bias=b2_sb[:, 0:1]).then_inc(h2_out_act, 1)

        @block.vector
        def _(dve):
            dve.memset(xt[:, :, :, N_SLOTS:PAD].rearrange("d t p s -> d (t p) s"), 0.0).then_inc(pad_zero, 1)
            dve.memset(packed[:, N_PACKED:], 0.0).then_inc(pairs_ready, 1)
            dve.wait_ge(row_ready, 1)
            dve.tensor_copy(row_f[:], row_of[:]).then_inc(row_ready, 1)
            dve.wait_ge(row_ready, 2)
            dve.wait_ge(id_rows_in, 16)
            for o in range(NO):
                b = o % 2
                if o >= 2:
                    dve.wait_ge(pick_done, o - 1)
                dve.tensor_copy(id16[0:OH_K, b], id_rows[0:OH_K, o]).then_inc(id16_ready, 1)
                dve.wait_ge(table_in[o % 3], 16 * (o // 3 + 1))
                dve.tensor_tensor(rest[0:OH_K, b], table[0:OH_K, o % 3], high_half(table[0:OH_K, o % 3]),
                                  ALU.subtract).then_inc(rest_ready, 1)
                dve.wait_ge(id16_ready, o + 1)
                for c in range(OH_CHUNKS):
                    dve.tensor_scalar(onehot[0:OH_K, b, c], id16[0:OH_K, b], row_f[0:OH_K, c:c + 1], None,
                                      ALU.is_equal)
                dve.wait_ge(rest_ready, o + 1)
                dve.tensor_tensor(low[0:OH_K, b], rest[0:OH_K, b], high_half(rest[0:OH_K, b]),
                                  ALU.subtract).then_inc(picks_ready, 1)
            dve.wait_ge(weights_in, 96)
            with dve.Fori(0, TILES) as t:
                for n in range(0, NT, 2):
                    w = len(bank_slots(n))
                    dve.wait_ge(tr_ready, t * NT + (n + 1))
                    if n == 0:
                        dve.tensor_copy(dense_t[:, t, :], tr_ps[0][:, 0, :])
                    dve.tensor_copy(tile_slots(t, n), group_order(tr_ps[0], w)).then_inc(tr_out_dve, 1)
                for s in range(SETS):
                    dve.wait_ge(gram_ready, t * SETS + (s + 1))
                    for q in (2, 3):
                        last = dve.tensor_copy(gram_block(s, q), gram_block_ps(s, q))
                    last.then_inc(gram_out_dve, 1)
                dve.wait_ge(gram_out_act, t * SETS + SETS)
                dve.wait_ge(gram_out_dve, t * SETS + SETS)
                dve.transpose(pairs[:].rearrange("p j i -> p (j i)"), gram_sb[:].rearrange("p j g -> p (j g)")
                              ).then_inc(pairs_ready, 1)
                dve.wait_ge(pairs_ready, t + 2)
                for r in range(len(RECTS)):
                    if r not in ACT_RECTS:
                        last = dve.tensor_copy(*rect(r))
                last.then_inc(packed_dve, 1)
                dve.wait_ge(back_ready, t + 1)
                dve.tensor_copy(pairs_t[:, 1:NC, :], dve_ps[:, 0:(NC - 1) * P]).then_inc(back_out_dve, 1)
                dve.wait_ge(h1_ready, t + 1)
                for m in (2, 3):
                    last = dve.tensor_scalar(h1[:, m, :], dve_ps[:, (m - 2) * P:(m - 1) * P], b1_sb[:, m:m + 1], 0.0,
                                             ALU.add, ALU.max)
                last.then_inc(h1_out_dve, 1)
                dve.wait_ge(h2_ready, t + 1)
                dve.tensor_scalar(h2[:, 1, :], dve_ps[:, 0:P], b2_sb[:, 1:2], 0.0,
                                  ALU.add, ALU.max).then_inc(h2_out_dve, 1)
                dve.wait_ge(y_ready, t + 1)
                dve.tensor_copy(y_sb[:, bass.ds(t, 1)], dve_ps[:, 0:1]).then_inc(y_out, 1)

        @block.tensor
        def _(pe):
            for o in range(NO):
                b = o % 2
                pe.wait_ge(picks_ready, o + 1)
                if o >= 2:
                    pe.wait_ge(pick_out, o - 1)
                for c in range(OH_CHUNKS):
                    parts = (high_half(table[0:OH_K, o % 3]), high_half(rest[0:OH_K, b]), low[0:OH_K, b])
                    for k, part in enumerate(parts):
                        last = pe.matmul(pick_ps[b][:], part[:, c, :], onehot[0:OH_K, b, c, :],
                                         start=(c == 0 and k == 0), stop=(c == OH_CHUNKS - 1 and k == 2))
                last.then_inc(pick_done, 1)

            pe.wait_ge(consts, 1)
            pe.wait_ge(dense_in, 16)
            for t in range(TILES):
                for n in range(NT):
                    pe.wait_ge(gathered[t][n], 16 * len([s for s in bank_slots(n) if s]))
                    before = t * ((NT + 1) // 2) + n // 2 if n % 2 == 0 else t * (NT // 2) + n // 2
                    if before:
                        pe.wait_ge(tr_out_dve if n % 2 == 0 else tr_out_act, before)
                    for s in bank_slots(n):
                        src = rows[:, t, s - 1, :] if s else dense_sb[:, t, :]
                        last = pe.transpose(tr_ps[n % 2][:, s % 4, :], src, ident[:])
                    last.then_inc(tr_ready, 1)

                pe.wait_ge(tr_out_dve, (t + 1) * ((NT + 1) // 2))
                pe.wait_ge(tr_out_act, (t + 1) * (NT // 2))
                if t == 0:
                    pe.wait_ge(pad_zero, 1)
                    pe.wait_ge(pick_out, NO)
                for s in range(SETS):
                    n = t * SETS + s
                    if n >= 2:
                        pe.wait_ge(gram_out_act, n - 1)
                        pe.wait_ge(gram_out_dve, n - 1)
                    for k in range(SET_G):
                        g = s * SET_G + k
                        group = xt[:, t, Q * g:Q * (g + 1), :]
                        last = pe.matmul(gram_ps[s % 2][:, k // 4, (k % 4) * Q * NJ:(k % 4 + 1) * Q * NJ],
                                         group, group[:, :, 1:N_SLOTS], start=True, stop=True)
                    last.then_inc(gram_ready, 1)

                pe.wait_ge(packed_act, t + 1)
                pe.wait_ge(packed_dve, t + 1)
                for c in range(NC):
                    last = pe.transpose(dve_ps[:, (c - 1) * P:c * P] if c else act_ps[:, 0:P], packed[:, c * P:(c + 1) * P], ident[:])
                last.then_inc(back_ready, 1)

                pe.wait_ge(back_out_act, t + 1)
                pe.wait_ge(back_out_dve, t + 1)
                if t == 0:
                    pe.wait_ge(weights_in, 96)
                for m in range(N1 // P):
                    dst = (act_ps if m < 2 else dve_ps)[:, m % 2 * P:(m % 2 + 1) * P]
                    pe.matmul(dst, w1d_sb[:, m * P:(m + 1) * P], dense_t[:, t, :], start=True, stop=False)
                    for c in range(NC):
                        last = pe.matmul(dst, w1p_sb[:, c, m * P:(m + 1) * P], pairs_t[:, c, :],
                                         start=False, stop=(c == NC - 1))
                last.then_inc(h1_ready, 1)

                pe.wait_ge(h1_out_act, t + 1)
                pe.wait_ge(h1_out_dve, t + 1)
                for m in range(N2 // P):
                    for c in range(N1 // P):
                        last = pe.matmul((act_ps, dve_ps)[m][:, 0:P], w2_sb[:, c, m * P:(m + 1) * P], h1[:, c, :],
                                         start=(c == 0), stop=(c == N1 // P - 1))
                last.then_inc(h2_ready, 1)

                pe.wait_ge(h2_out_act, t + 1)
                pe.wait_ge(h2_out_dve, t + 1)
                for c in range(N2 // P):
                    last = pe.matmul(dve_ps[:, 0:1], h2[:, c, :], w3_sb[:, c:c + 1], start=(c == 0),
                                     stop=(c == N2 // P - 1))
                last.then_inc(y_ready, 1)


def pair_row(i, j):
    a, b = sorted((SLOT_FIELD[i], SLOT_FIELD[j]))
    return a * (2 * N_SLOTS - a - 1) // 2 + (b - a - 1)


def kernel(**inputs):
    import concourse.bacc as bacc
    from concourse.bass_utils import run_bass_kernel_spmd as run

    a = {k: np.ascontiguousarray(v) for k, v in inputs.items()}
    w1 = a["W_top1"]
    n_pairs = N_SLOTS * (N_SLOTS - 1) // 2
    w1_pairs = np.zeros((P, NC, N1), w1.dtype)
    for r, (j0, nj) in enumerate(RECTS):
        for j in range(j0, j0 + nj):
            for i in range(j):
                c, k = divmod(rect_at(r) + (j - j0) * (j0 + nj - 1) + i, P)
                w1_pairs[k, c] = w1[pair_row(i, j)]
    laid = {
        "dense": a["r_dense_x"],
        "ids": a["ids"],
        "ids_by_field": np.ascontiguousarray(
            a["ids"].reshape(Q, G, TILES, N_FIELDS).transpose(3, 2, 1, 0).reshape(N_FIELDS, B)[ONEHOT]),
        "w1_pairs": w1_pairs,
        "w1_dense": np.ascontiguousarray(w1[n_pairs:]),
        "b1": np.ascontiguousarray(a["b_top1"].reshape(N1 // P, P).T),
        "w2": a["W_top2"],
        "b2": np.ascontiguousarray(a["b_top2"].reshape(N2 // P, P).T),
        "w3": np.ascontiguousarray(a["W_top3"].reshape(N2 // P, P).T),
    }
    for f in range(N_FIELDS):
        laid[f"table{f}"] = a[f"tbl_{f}"]

    nc = bacc.Bacc("TRN2", target_bir_lowering=False, num_devices=1)
    ap = {k: nc.dram_tensor(k, v.shape, mybir.dt.from_np(v.dtype), kind="ExternalInput").ap() for k, v in laid.items()}
    out = nc.dram_tensor("y", (B, 1), F32, kind="ExternalOutput").ap()
    tower(nc, ap["dense"], ap["ids"], ap["ids_by_field"], [ap[f"table{f}"] for f in range(N_FIELDS)],
          ap["w1_pairs"], ap["w1_dense"], ap["b1"], ap["w2"], ap["b2"], ap["w3"], out)
    return run(nc, [laid], core_ids=[0]).results[0]["y"]
```

```python
from contextlib import ExitStack

import numpy as np

import concourse.bass as bass
from concourse import mybir

P = 128
B = 512
D = 128
N_FIELDS = 26
N_SLOTS = 27
N1, N2 = 512, 256
TILES = B // P
Q = 4
G = P // Q
PAD = 32

ONEHOT = [0, 4, 7, 11, 12, 13, 15]
OH_CHUNKS = 8
OH_K = 1000 // OH_CHUNKS
GATHERED = [f for f in range(N_FIELDS) if f not in ONEHOT]
NG = len(GATHERED)
NO = len(ONEHOT)
SLOT_FIELD = [N_FIELDS] + GATHERED + ONEHOT
NT = -(-NG // 4)
TR_OUT = [(NT + 1) // 2, NT // 2]
WARM_UP = 9
TABLES = 2
WEIGHTS = 6 * 16
NJ = N_SLOTS - 1
SET_G = 4
SETS = G // SET_G
GRAM_BANKS = 3
RECTS = [(1, 2)] + [(j, 3) for j in range(3, N_SLOTS, 3)]
NC = 3


def rect_at(r):
    return sum(nj * (j0 + nj - 1) for j0, nj in RECTS[:r])


N_PACKED = rect_at(len(RECTS))
assert N_PACKED <= NC * P
ACT_RECTS = [8, 7, 6]

ALU = mybir.AluOpType
ACT = mybir.ActivationFunctionType
F32 = mybir.dt.float32
F16 = mybir.dt.float16
F32R = mybir.dt.float32r
BF16 = mybir.dt.bfloat16
I32 = mybir.dt.int32


def tower(nc, dense, ids, ids_by_field, tables, w1_pairs, w1_dense, b1, w2, b2, w3, out):
    with ExitStack() as ctx:
        def sb(name, shape, dt=F32):
            return ctx.enter_context(nc.sbuf_tensor(name, shape, dt))

        def psum(name, shape):
            return ctx.enter_context(nc.psum_tensor(name, shape, F32))

        def sem(name):
            return ctx.enter_context(nc.semaphore(name))

        ids_sb = sb("ids_sb", [P, TILES, N_FIELDS], I32)
        dense_sb = sb("dense_sb", [P, TILES, D])
        rows = sb("rows", [P, TILES, NG, D])
        xt = sb("xt", [P, TILES, P, PAD])
        dense_t = sb("dense_t", [P, TILES, P])
        gram_sb = sb("gram_sb", [P, NJ, G])
        pairs = sb("pairs", [P, NJ, PAD])
        packed = sb("packed", [P, NC * P])
        pairs_t = sb("pairs_t", [P, NC, P])
        h1 = sb("h1", [P, N1 // P, P])
        h2 = sb("h2", [P, N2 // P, P])
        y_sb = sb("y_sb", [P, TILES])
        w1p_sb = sb("w1p_sb", [P, NC, N1])
        w1d_sb = sb("w1d_sb", [P, N1])
        w2_sb = sb("w2_sb", [P, N1 // P, N2])
        w3_sb = sb("w3_sb", [P, N2 // P])
        b1_sb = sb("b1_sb", [P, N1 // P])
        b2_sb = sb("b2_sb", [P, N2 // P])
        ident = sb("ident", [P, P])
        zeros = sb("zeros", [P, B], BF16)
        row_of = sb("row_of", [P, OH_CHUNKS], I32)
        row_f = sb("row_f", [P, OH_CHUNKS])
        id_rows = sb("id_rows", [P, NO, B], I32)
        id16 = sb("id16", [P, 2, B], F16)
        onehot = sb("onehot", [P, 2, OH_CHUNKS, B], F32R)
        table = sb("table", [P, TABLES, OH_CHUNKS, D])
        high = sb("high", [P, 2, OH_CHUNKS, D], F32R)
        low = sb("low", [P, 2, OH_CHUNKS, D], F32R)

        tr_ps = [psum(f"tr_ps{i}", [P, 4, P]) for i in range(2)]
        gram_ps = [psum(f"gram_ps{i}", [P, 512]) for i in range(GRAM_BANKS)]
        act_ps = psum("act_ps", [P, 512])
        dve_ps = psum("dve_ps", [P, 512])
        top_ps = psum("top_ps", [P, 4, P])
        pick_ps = gram_ps[1:]
        h1_ps = [act_ps[:, 0:P], act_ps[:, P:2 * P], dve_ps[:, 0:P], dve_ps[:, P:2 * P]]
        h1_ps_last = [act_ps[:, 0:P], tr_ps[1][:, 0, :], dve_ps[:, 0:P], tr_ps[0][:, 0, :]]
        h2_ps = [top_ps[:, 0, :], top_ps[:, 1, :]]
        h2_ps_last = [act_ps[:, 0:P], dve_ps[:, 0:P]]
        y_ps = top_ps[:, 2, 0:1]

        ids_in = sem("ids_in")
        dense_in = sem("dense_in")
        weights_in = sem("weights_in")
        id_row_in = [sem(f"id_row_in{o}") for o in range(NO)]
        table_in = [sem(f"table_in{i}") for i in range(TABLES)]
        gathered = [[sem(f"gathered{t}_{n}") for n in range(NT)] for t in range(TILES)]
        zeros_ready = sem("zeros_ready")
        ident_zero = sem("ident_zero")
        ident_ready = sem("ident_ready")
        row_ready = sem("row_ready")
        pad_zero = sem("pad_zero")
        id16_ready = sem("id16_ready")
        high_ready = sem("high_ready")
        onehot_ready = sem("onehot_ready")
        low_ready = sem("low_ready")
        pick_done = sem("pick_done")
        pick_out = sem("pick_out")
        dense_ready = sem("dense_ready")
        dense_out = sem("dense_out")
        tr_ready = sem("tr_ready")
        tr_out_dve = sem("tr_out_dve")
        tr_out_act = sem("tr_out_act")
        gram_ready = sem("gram_ready")
        gram_out_dve = sem("gram_out_dve")
        gram_out_act = sem("gram_out_act")
        pairs_ready = sem("pairs_ready")
        packed_dve = sem("packed_dve")
        packed_act = sem("packed_act")
        back_ready = sem("back_ready")
        back_out_dve = sem("back_out_dve")
        back_out_act = sem("back_out_act")
        h1_ready = sem("h1_ready")
        h1_out_dve = sem("h1_out_dve")
        h1_out_act = sem("h1_out_act")
        h2_ready = sem("h2_ready")
        h2_out_dve = sem("h2_out_dve")
        h2_out_act = sem("h2_out_act")
        y_ready = sem("y_ready")
        y_out = sem("y_out")
        stored = sem("stored")

        block = ctx.enter_context(nc.Block())

        def bank_slots(n):
            return range(4 * n + 1, min(4 * n + 4, NG) + 1)

        def gram_block(s, q):
            return gram_sb[PAD * q:PAD * q + NJ, :, s * SET_G:(s + 1) * SET_G]

        def gram_block_ps(s, q):
            v = gram_ps[s % GRAM_BANKS][PAD * q:PAD * q + NJ, 0:SET_G * Q * NJ].rearrange("i (g n) -> i g n", g=SET_G)
            return v[:, :, q * NJ:(q + 1) * NJ].rearrange("i g j -> i j g")

        def high_half(ap):
            v = ap.bitcast(BF16)
            return v.rearrange("p c (d h) -> p c d h", h=2)[:, :, :, 1]

        def group_order(bank, w):
            return bank[:, 0:w, :].rearrange("d s (q g) -> d g q s", q=Q)

        def tile_slots(t, n):
            w = len(bank_slots(n))
            return xt[:, t, :, 4 * n + 1:4 * n + 1 + w].rearrange("d (g q) s -> d g q s", q=Q)

        def rect(r):
            j0, nj = RECTS[r]
            ni = j0 + nj - 1
            to = packed[:, rect_at(r):rect_at(r) + nj * ni].rearrange("p (j i) -> p j i", j=nj)
            return to, pairs[:, j0 - 1:j0 - 1 + nj, 0:ni]

        @block.sync
        def _(sp):
            for o in range(NO):
                sp.dma_start(id_rows[0:OH_K, o], ids_by_field[o:o + 1].to_broadcast([OH_K, B])).then_inc(id_row_in[o], 16)
                if o >= TABLES:
                    sp.wait_ge(low_ready, o - TABLES + 1)
                sp.dma_start(table[0:OH_K, o % TABLES], tables[ONEHOT[o]].rearrange("(p c) d -> p c d", c=OH_CHUNKS)
                             ).then_inc(table_in[o % TABLES], 16)
                if o == TABLES - 1:
                    sp.dma_start(dense_sb[:], dense.rearrange("(p t) d -> p t d", t=TILES)).then_inc(dense_in, 16)
                    sp.dma_start(w1p_sb[:], w1_pairs).then_inc(weights_in, 16)
                    sp.dma_start(w1d_sb[:], w1_dense).then_inc(weights_in, 16)
                    sp.dma_start(w2_sb[:], w2.rearrange("(c k) n -> k c n", k=P)).then_inc(weights_in, 16)
                    sp.dma_start(w3_sb[:], w3).then_inc(weights_in, 16)
                    sp.dma_start(b1_sb[:], b1).then_inc(weights_in, 16)
                    sp.dma_start(b2_sb[:], b2).then_inc(weights_in, 16)
            sp.wait_ge(y_out, TILES)
            sp.dma_start(out.rearrange("(p t) o -> p (t o)", t=TILES), y_sb[:]).then_inc(stored, 16)
            sp.wait_ge(stored, 16)

        @block.gpsimd
        def _(pool):
            pool.memset(ident[:], 0.0).then_inc(ident_zero, 1)
            pool.iota(row_of[:], pattern=[[1, OH_CHUNKS]], base=0, channel_multiplier=OH_CHUNKS).then_inc(row_ready, 1)
            pool.wait_ge(ident_zero, 1)
            pool.affine_select(out=ident[:], in_=ident[:], compare_op=ALU.not_equal, fill=1.0, base=0,
                               pattern=[[-1, P]], channel_multiplier=1).then_inc(ident_ready, 1)
            pool.wait_ge(ids_in, 16)
            for t in range(TILES):
                for s in range(1, NG + 1):
                    f = SLOT_FIELD[s]
                    pool.indirect_dma_start(rows[:, t, s - 1, :], None, tables[f],
                                            bass.IndirectOffsetOnAxis(ids_sb[:, t, f:f + 1], 0)
                                            ).then_inc(gathered[t][(s - 1) // 4], 16)


        @block.scalar
        def _(act):
            act.dma_start(ids_sb[:], ids.rearrange("(p t) f -> p t f", t=TILES)).then_inc(ids_in, 16)
            def picked(o):
                act.wait_ge(pick_done, o + 1)
                act.activation(xt[:, :, :, NG + 1 + o], pick_ps[o % 2][:].rearrange("d (t p) -> d t p", t=TILES),
                               ACT.Copy).then_inc(pick_out, 1)

            def transposed(t, banks):
                for n in banks:
                    if n % 2 == 1:
                        act.wait_ge(tr_ready, t * NT + (n + 1))
                        act.activation(tile_slots(t, n), group_order(tr_ps[1], len(bank_slots(n))), ACT.Copy
                                       ).then_inc(tr_out_act, 1)

            def gram(t):
                for s in range(SETS):
                    act.wait_ge(gram_ready, t * SETS + (s + 1))
                    for q in (0, 1):
                        last = act.activation(gram_block(s, q), gram_block_ps(s, q), ACT.Copy)
                    last.then_inc(gram_out_act, 1)

            def back(n):
                act.wait_ge(back_ready, n)
                act.activation(pairs_t[:, 0, :], gram_ps[0][:, 0:P], ACT.Copy).then_inc(back_out_act, 1)

            def first_layer(n):
                act.wait_ge(h1_ready, n * (N1 // P))
                for m in (0, 1):
                    act.activation(h1[:, m, :], h1_ps[m], ACT.Relu, bias=b1_sb[:, m:m + 1]).then_inc(h1_out_act, 1)

            def second_layer(n):
                act.wait_ge(h2_ready, n)
                for m in (0, 1):
                    last = act.activation(h2[:, m, :], h2_ps[m], ACT.Relu, bias=b2_sb[:, m:m + 1])
                last.then_inc(h2_out_act, 1)

            def third_layer(n):
                act.wait_ge(y_ready, n)
                act.activation(y_sb[:, bass.ds(n - 1, 1)], y_ps, ACT.Copy).then_inc(y_out, 1)

            def pack(n):
                act.wait_ge(pairs_ready, n + 1)
                for r in ACT_RECTS:
                    last = act.activation(*rect(r), ACT.Copy)
                last.then_inc(packed_act, 1)

            def step(t, third):
                transposed(t, (0, 1))
                pack(t)
                if third:
                    second_layer(t - 1)
                back(t)
                transposed(t, (2, 3))
                if third:
                    third_layer(t - 1)
                transposed(t, range(4, NT))
                first_layer(t)
                gram(t)

            def split(o):
                if o >= 2:
                    act.wait_ge(pick_done, o - 1)
                act.wait_ge(table_in[o % TABLES], 16 * (o // TABLES + 1))
                act.activation(high[0:OH_K, o % 2], table[0:OH_K, o % TABLES], ACT.Copy).then_inc(high_ready, 1)

            split(0)
            split(1)
            picked(0)
            split(2)
            picked(1)
            split(3)
            act.wait_ge(dense_ready, 1)
            act.activation(xt[:, :, :, 0].rearrange("d t (g q) -> d t g q", q=Q),
                           tr_ps[0][:, :, :].rearrange("d t (q g) -> d t g q", q=Q), ACT.Copy)
            act.activation(dense_t[:], tr_ps[0][:, :, :], ACT.Copy).then_inc(dense_out, 1)
            for o in range(2, NO - 1):
                picked(o)
                if o + 2 < NO:
                    split(o + 2)
            transposed(0, range(NT))
            picked(NO - 1)
            act.wait_ge(pairs_ready, 1)
            gram(0)
            act.wait_ge(weights_in, WEIGHTS)
            step(1, False)
            with act.Fori(2, TILES) as t:
                step(t, True)
            pack(TILES)
            second_layer(TILES - 1)
            back(TILES)
            third_layer(TILES - 1)
            for k, m in enumerate((0, 1)):
                act.wait_ge(h1_ready, (TILES - 1) * (N1 // P) + 2 * k + 1)
                act.activation(h1[:, m, :], h1_ps_last[m], ACT.Relu, bias=b1_sb[:, m:m + 1]).then_inc(h1_out_act, 1)
            act.wait_ge(h2_ready, TILES)
            act.activation(h2[:, 0, :], h2_ps_last[0], ACT.Relu, bias=b2_sb[:, 0:1]).then_inc(h2_out_act, 1)
            third_layer(TILES)

        @block.vector
        def _(dve):
            dve.memset(zeros[:], 0.0).then_inc(zeros_ready, 1)
            dve.memset(xt[:, :, :, N_SLOTS:PAD].rearrange("d t p s -> d (t p) s"), 0.0).then_inc(pad_zero, 1)
            dve.memset(packed[:, N_PACKED:], 0.0)
            dve.memset(gram_sb[:], 0.0).then_inc(pairs_ready, 1)
            dve.wait_ge(row_ready, 1)
            dve.tensor_copy(row_f[:], row_of[:]).then_inc(row_ready, 1)
            dve.wait_ge(row_ready, 2)
            for o in range(NO):
                b = o % 2
                dve.wait_ge(id_row_in[o], 16)
                if o >= 2:
                    dve.wait_ge(pick_done, o - 1)
                dve.tensor_copy(id16[0:OH_K, b], id_rows[0:OH_K, o]).then_inc(id16_ready, 1)
                dve.wait_ge(id16_ready, o + 1)
                for c in range(OH_CHUNKS):
                    dve.tensor_scalar(onehot[0:OH_K, b, c], id16[0:OH_K, b], row_f[0:OH_K, c:c + 1], None,
                                      ALU.is_equal).then_inc(onehot_ready, 1)
                dve.wait_ge(high_ready, o + 1)
                dve.tensor_tensor(low[0:OH_K, b], table[0:OH_K, o % TABLES], high[0:OH_K, b].bitcast(F32),
                                  ALU.subtract).then_inc(low_ready, 1)

            def transposed(t, banks):
                for n in banks:
                    if n % 2 == 0:
                        dve.wait_ge(tr_ready, t * NT + (n + 1))
                        dve.tensor_copy(tile_slots(t, n), group_order(tr_ps[0], len(bank_slots(n)))
                                        ).then_inc(tr_out_dve, 1)

            def gram(t):
                for s in range(SETS):
                    dve.wait_ge(gram_ready, t * SETS + (s + 1))
                    for q in (2, 3):
                        last = dve.tensor_copy(gram_block(s, q), gram_block_ps(s, q))
                    last.then_inc(gram_out_dve, 1)

            def squares(n):
                dve.wait_ge(gram_out_act, n * SETS)
                dve.wait_ge(gram_out_dve, n * SETS)
                dve.transpose(pairs[:].rearrange("p j i -> p (j i)"), gram_sb[:].rearrange("p j g -> p (j g)")
                              ).then_inc(pairs_ready, 1)

            def pack(n):
                dve.wait_ge(pairs_ready, n + 1)
                for r in range(len(RECTS)):
                    if r not in ACT_RECTS:
                        last = dve.tensor_copy(*rect(r))
                last.then_inc(packed_dve, 1)

            def back(n):
                dve.wait_ge(back_ready, n)
                dve.tensor_copy(pairs_t[:, 1:NC, :].rearrange("k c p -> k (c p)"), gram_ps[1][:, 0:(NC - 1) * P]
                                ).then_inc(back_out_dve, 1)

            def first_layer(n):
                dve.wait_ge(h1_ready, n * (N1 // P))
                for m in (2, 3):
                    dve.tensor_scalar(h1[:, m, :], h1_ps[m], b1_sb[:, m:m + 1], 0.0, ALU.add, ALU.max
                                      ).then_inc(h1_out_dve, 1)

            transposed(0, range(NT))
            gram(0)
            dve.wait_ge(weights_in, WEIGHTS)
            with dve.Fori(1, TILES) as t:
                squares(t)
                pack(t)
                transposed(t, (0, 1))
                back(t)
                transposed(t, range(2, NT))
                first_layer(t)
                gram(t)
            squares(TILES)
            pack(TILES)
            back(TILES)
            for k, m in enumerate((2, 3)):
                dve.wait_ge(h1_ready, (TILES - 1) * (N1 // P) + 2 * k + 2)
                dve.tensor_scalar(h1[:, m, :], h1_ps_last[m], b1_sb[:, m:m + 1], 0.0, ALU.add, ALU.max
                                  ).then_inc(h1_out_dve, 1)
            dve.wait_ge(h2_ready, TILES)
            dve.tensor_scalar(h2[:, 1, :], h2_ps_last[1], b2_sb[:, 1:2], 0.0, ALU.add, ALU.max
                              ).then_inc(h2_out_dve, 1)

        @block.tensor
        def _(pe):

            def pick(o, part):
                b = o % 2
                if part == 0:
                    if o >= 2:
                        pe.wait_ge(pick_out, o - 1)
                    pe.wait_ge(high_ready, o + 1)
                    weights = high[0:OH_K, b]
                else:
                    pe.wait_ge(low_ready, o + 1)
                    weights = low[0:OH_K, b]
                for c in range(OH_CHUNKS):
                    if part == 0:
                        pe.wait_ge(onehot_ready, OH_CHUNKS * o + c + 1)
                    last = pe.matmul(pick_ps[b][:], weights[:, c, :], onehot[0:OH_K, b, c, :],
                                     start=(c == 0 and part == 0), stop=(c == OH_CHUNKS - 1 and part == 1))
                if part == 1:
                    last.then_inc(pick_done, 1)

            def transposes(t, banks):
                for n in banks:
                    pe.wait_ge(gathered[t][n], 16 * len(bank_slots(n)))
                    out_of = (tr_out_dve, tr_out_act)[n % 2]
                    before = t * TR_OUT[n % 2] + n // 2
                    if before:
                        pe.wait_ge(out_of, before)
                    elif n == 0:
                        pe.wait_ge(dense_out, 1)
                    for s in bank_slots(n):
                        last = pe.transpose(tr_ps[n % 2][:, (s - 1) % 4, :], rows[:, t, s - 1, :], ident[:])
                    last.then_inc(tr_ready, 1)

            def gram(t):
                pe.wait_ge(tr_out_dve, (t + 1) * TR_OUT[0])
                pe.wait_ge(tr_out_act, (t + 1) * TR_OUT[1])
                for s in range(SETS):
                    if s >= GRAM_BANKS:
                        pe.wait_ge(gram_out_act, t * SETS + s - GRAM_BANKS + 1)
                        pe.wait_ge(gram_out_dve, t * SETS + s - GRAM_BANKS + 1)
                    for k in range(SET_G):
                        g = s * SET_G + k
                        group = xt[:, t, Q * g:Q * (g + 1), :]
                        weights = group.rearrange("d q i -> d (q i)")[:, 0:(Q - 1) * PAD + NJ]
                        last = pe.matmul(gram_ps[s % GRAM_BANKS][0:(Q - 1) * PAD + NJ, k * Q * NJ:(k + 1) * Q * NJ],
                                         weights, group[:, :, 1:N_SLOTS], start=True, stop=True)
                    last.then_inc(gram_ready, 1)

            def dense_part(t):
                if t:
                    pe.wait_ge(h1_out_act, 2 * t)
                    pe.wait_ge(h1_out_dve, 2 * t)
                ps = h1_banks(t)
                for m in range(N1 // P):
                    pe.matmul(ps[m], w1d_sb[:, m * P:(m + 1) * P], dense_t[:, t, :],
                              start=(m % 2 == 0 or t == TILES - 1), stop=False, skip_group_check=True)

            def back(t):
                pe.wait_ge(packed_act, t + 1)
                pe.wait_ge(packed_dve, t + 1)
                for c in range(NC):
                    last = pe.transpose(gram_ps[1][:, (c - 1) * P:c * P] if c else gram_ps[0][:, 0:P],
                                        packed[:, c * P:(c + 1) * P], ident[:])
                last.then_inc(back_ready, 1)

            def h1_banks(t):
                return h1_ps_last if t == TILES - 1 else h1_ps

            def first_layer(t, parts):
                pe.wait_ge(back_out_act, t + 1)
                pe.wait_ge(back_out_dve, t + 1)
                for m in parts:
                    for c in range(NC):
                        last = pe.matmul(h1_banks(t)[m], w1p_sb[:, c, m * P:(m + 1) * P], pairs_t[:, c, :],
                                         start=False, stop=(c == NC - 1), skip_group_check=True)
                    last.then_inc(h1_ready, 1)

            def second_layer(t):
                if t:
                    pe.wait_ge(y_out, t)
                pe.wait_ge(h1_out_act, 2 * t + 2)
                pe.wait_ge(h1_out_dve, 2 * t + 2)
                for m in range(N2 // P):
                    for c in range(N1 // P):
                        last = pe.matmul(h2_ps[m], w2_sb[:, c, m * P:(m + 1) * P], h1[:, c, :],
                                         start=(c == 0), stop=(c == N1 // P - 1))
                last.then_inc(h2_ready, 1)

            def second_layer_last(t):
                for k, c in enumerate((0, 2, 1, 3)):
                    pe.wait_ge((h1_out_act, h1_out_dve)[c // 2], 2 * t + 1 + k // 2)
                    if k == 0:
                        pe.wait_ge(h1_out_dve, 2 * t + 1)
                    for m in range(N2 // P):
                        last = pe.matmul(h2_ps_last[m], w2_sb[:, c, m * P:(m + 1) * P], h1[:, c, :],
                                         start=(k == 0), stop=(k == 3))
                last.then_inc(h2_ready, 1)

            def third_layer(t):
                pe.wait_ge(h2_out_act, t + 1)
                if t == TILES - 1:
                    pe.wait_ge(h2_out_dve, 1)
                    pe.wait_ge(y_out, t)
                for c in range(N2 // P):
                    last = pe.matmul(y_ps, h2[:, c, :], w3_sb[:, c:c + 1], start=(c == 0),
                                     stop=(c == N2 // P - 1))
                last.then_inc(y_ready, 1)

            pe.wait_ge(zeros_ready, 1)
            for _ in range(WARM_UP):
                pe.matmul(act_ps[:], zeros[:, 0:P], zeros[:], start=True, stop=True)

            for o in range(NO - 1):
                for part in range(2):
                    pick(o, part)
                if o == 1:
                    pe.wait_ge(ident_ready, 1)
                    pe.wait_ge(dense_in, 16)
                    for t in range(TILES):
                        last = pe.transpose(tr_ps[0][:, t, :], dense_sb[:, t, :], ident[:])
                    last.then_inc(dense_ready, 1)
            transposes(0, (0, 1))
            pick(NO - 1, 0)
            transposes(0, (2, 3))
            transposes(0, range(4, NT))
            pick(NO - 1, 1)
            pe.wait_ge(weights_in, WEIGHTS)
            dense_part(0)
            pe.wait_ge(pad_zero, 1)
            pe.wait_ge(pick_out, NO)
            gram(0)
            for t in range(1, TILES):
                transposes(t, (0, 1))
                if t >= 2:
                    dense_part(t - 1)
                    second_layer(t - 2)
                back(t - 1)
                transposes(t, (2, 3))
                if t >= 2:
                    third_layer(t - 2)
                first_layer(t - 1, (0, 2))
                transposes(t, range(4, NT))
                first_layer(t - 1, (1, 3))
                gram(t)
            dense_part(TILES - 1)
            second_layer(TILES - 2)
            back(TILES - 1)
            third_layer(TILES - 2)
            first_layer(TILES - 1, (0, 2, 1, 3))
            second_layer_last(TILES - 1)
            third_layer(TILES - 1)


def pair_row(i, j):
    a, b = sorted((SLOT_FIELD[i], SLOT_FIELD[j]))
    return a * (2 * N_SLOTS - a - 1) // 2 + (b - a - 1)


def kernel(**inputs):
    import concourse.bacc as bacc
    from concourse.bass_utils import run_bass_kernel_spmd as run

    a = {k: np.ascontiguousarray(v) for k, v in inputs.items()}
    w1 = a["W_top1"]
    n_pairs = N_SLOTS * (N_SLOTS - 1) // 2
    w1_pairs = np.zeros((P, NC, N1), w1.dtype)
    for r, (j0, nj) in enumerate(RECTS):
        for j in range(j0, j0 + nj):
            for i in range(j):
                c, k = divmod(rect_at(r) + (j - j0) * (j0 + nj - 1) + i, P)
                w1_pairs[k, c] = w1[pair_row(i, j)]
    laid = {
        "dense": a["r_dense_x"],
        "ids": a["ids"],
        "ids_by_field": np.ascontiguousarray(
            a["ids"].reshape(Q, G, TILES, N_FIELDS).transpose(3, 2, 1, 0).reshape(N_FIELDS, B)[ONEHOT]),
        "w1_pairs": w1_pairs,
        "w1_dense": np.ascontiguousarray(w1[n_pairs:]),
        "b1": np.ascontiguousarray(a["b_top1"].reshape(N1 // P, P).T),
        "w2": a["W_top2"],
        "b2": np.ascontiguousarray(a["b_top2"].reshape(N2 // P, P).T),
        "w3": np.ascontiguousarray(a["W_top3"].reshape(N2 // P, P).T),
    }
    for f in range(N_FIELDS):
        laid[f"table{f}"] = a[f"tbl_{f}"]

    nc = bacc.Bacc("TRN2", target_bir_lowering=False, num_devices=1)
    ap = {k: nc.dram_tensor(k, v.shape, mybir.dt.from_np(v.dtype), kind="ExternalInput").ap() for k, v in laid.items()}
    out = nc.dram_tensor("y", (B, 1), F32, kind="ExternalOutput").ap()
    tower(nc, ap["dense"], ap["ids"], ap["ids_by_field"], [ap[f"table{f}"] for f in range(N_FIELDS)],
          ap["w1_pairs"], ap["w1_dense"], ap["b1"], ap["w2"], ap["b2"], ap["w3"], out)
    return run(nc, [laid], core_ids=[0]).results[0]["y"]
```

```python
from contextlib import ExitStack

import numpy as np

import concourse.bass as bass
from concourse import mybir

P = 128
B = 512
D = 128
N_FIELDS = 26
N_SLOTS = 27
N1, N2 = 512, 256
TILES = B // P
Q = 4
G = P // Q
PAD = 32

ONEHOT = [0, 4, 7, 11, 12, 13, 15]
OH_CHUNKS = 8
OH_K = 1000 // OH_CHUNKS
LATE = 17
GATHERED = [LATE] + [f for f in range(N_FIELDS) if f not in ONEHOT + [LATE]]
NG = len(GATHERED)
NO = len(ONEHOT)
SLOT_FIELD = [N_FIELDS] + GATHERED + ONEHOT
FULL_BANKS = (NG - 1) // 4
BANK_SLOTS = [range(4 * n + 1, 4 * n + 5) for n in range(FULL_BANKS)]
BANK_SLOTS += [slots for slots in (range(4 * FULL_BANKS + 1, NG), range(NG, NG + 1)) if slots]
NT = len(BANK_SLOTS)
TR_OUT = [(NT + 1) // 2, NT // 2]
DVE_CHUNKS = ((0, 1), (2, 3, 4))
SHARED = 5
SHARED_COLS = 192
ACT_COLS = (OH_CHUNKS - SHARED) * B - SHARED_COLS
WARM_UP = (8, 8)
TABLES = 2
WEIGHTS = 6 * 16
NJ = N_SLOTS - 1
SET_G = 4
SETS = G // SET_G
GRAM_BANKS = 3
RECTS = [(1, 2)] + [(j, 3) for j in range(3, N_SLOTS, 3)]
NC = 3


def rect_at(r):
    return sum(nj * (j0 + nj - 1) for j0, nj in RECTS[:r])


N_PACKED = rect_at(len(RECTS))
assert N_PACKED <= NC * P
ACT_RECTS_EARLY = [8, 7, 6]
ACT_RECTS_LATE = [5, 4]
EARLY_J = RECTS[6][0] - 1

ALU = mybir.AluOpType
ACT = mybir.ActivationFunctionType
F32 = mybir.dt.float32
F16 = mybir.dt.float16
F32R = mybir.dt.float32r
BF16 = mybir.dt.bfloat16
I32 = mybir.dt.int32


def tower(nc, dense, ids, ids_by_field, tables, w1_pairs, w1_dense, b1, w2, b2, w3, out):
    with ExitStack() as ctx:
        def sb(name, shape, dt=F32):
            return ctx.enter_context(nc.sbuf_tensor(name, shape, dt))

        def psum(name, shape):
            return ctx.enter_context(nc.psum_tensor(name, shape, F32))

        def sem(name):
            return ctx.enter_context(nc.semaphore(name))

        ids_sb = sb("ids_sb", [P, TILES, N_FIELDS], I32)
        dense_sb = sb("dense_sb", [P, TILES, D])
        rows = sb("rows", [P, TILES, NG, D])
        xt = sb("xt", [P, TILES, P, PAD])
        dense_t = sb("dense_t", [P, TILES, P])
        gram_sb = sb("gram_sb", [P, NJ, G])
        pairs = sb("pairs", [P, NJ, PAD])
        packed = sb("packed", [P, NC * P])
        pairs_t = sb("pairs_t", [P, NC, P])
        h1 = sb("h1", [P, N1 // P, P])
        h2 = sb("h2", [P, N2 // P, P])
        y_sb = sb("y_sb", [P, TILES])
        w1p_sb = sb("w1p_sb", [P, NC, N1])
        w1d_sb = sb("w1d_sb", [P, N1])
        w2_sb = sb("w2_sb", [P, N1 // P, N2])
        w3_sb = sb("w3_sb", [P, N2 // P])
        b1_sb = sb("b1_sb", [P, N1 // P])
        b2_sb = sb("b2_sb", [P, N2 // P])
        ident = sb("ident", [P, P])
        zeros = sb("zeros", [P, B], BF16)
        row_of = sb("row_of", [P, OH_CHUNKS], I32)
        field_of = sb("field_of", [NO + 1, NO + 1], I32)
        row_f = sb("row_f", [P, OH_CHUNKS])
        row_neg = sb("row_neg", [P, OH_CHUNKS])
        field_ids = sb("field_ids", [NO + 1, B], I32)
        field_ids16 = sb("field_ids16", [NO + 1, B], F16)
        select = sb("select", [NO + 1, NO + 1, OH_K], F16)
        distance = sb("distance", [P, ACT_COLS])
        onehot = sb("onehot", [P, 2, OH_CHUNKS, B], F32R)
        table = sb("table", [P, TABLES, OH_CHUNKS, D])
        high = sb("high", [P, 2, OH_CHUNKS, D], F32R)
        low = sb("low", [P, 2, OH_CHUNKS, D], F32R)

        tr_ps = [psum(f"tr_ps{i}", [P, 4, P]) for i in range(2)]
        gram_ps = [psum(f"gram_ps{i}", [P, 512]) for i in range(GRAM_BANKS)]
        act_ps = psum("act_ps", [P, 512])
        dve_ps = psum("dve_ps", [P, 512])
        top_ps = psum("top_ps", [P, 4, P])
        pick_ps = gram_ps[1:]
        ids_ps_dve = [dve_ps, gram_ps[0]]
        ids_ps_act = [act_ps[:], top_ps[:].rearrange("p c n -> p (c n)")]
        h1_ps = [act_ps[:, 0:P], act_ps[:, P:2 * P], dve_ps[:, 0:P], dve_ps[:, P:2 * P]]
        h1_ps_last = [act_ps[:, 0:P], tr_ps[1][:, 0, :], dve_ps[:, 0:P], tr_ps[0][:, 0, :]]
        late_ids_ps = top_ps[:, 0, :]
        late_ps = top_ps[:, 3, :]
        h2_ps = [top_ps[:, 0, :], top_ps[:, 1, :]]
        h2_ps_last = [act_ps[:, 0:P], dve_ps[:, 0:P]]
        y_ps = top_ps[:, 2, 0:1]

        ids_in = sem("ids_in")
        dense_in = sem("dense_in")
        weights_in = sem("weights_in")
        field_ids_in = sem("field_ids_in")
        table_in = [sem(f"table_in{i}") for i in range(TABLES)]
        gathered = [[sem(f"gathered{t}_{n}") for n in range(NT)] for t in range(TILES)]
        zeros_ready = sem("zeros_ready")
        ident_zero = sem("ident_zero")
        ident_ready = sem("ident_ready")
        row_ready = sem("row_ready")
        pad_zero = sem("pad_zero")
        row_f_ready = sem("row_f_ready")
        row_neg_ready = sem("row_neg_ready")
        select_ready = sem("select_ready")
        ids16_ready = sem("ids16_ready")
        ids_spread = sem("ids_spread")
        distance_ready = sem("distance_ready")
        high_ready = sem("high_ready")
        onehot_dve = sem("onehot_dve")
        onehot_act = sem("onehot_act")
        low_ready = sem("low_ready")
        pick_done = sem("pick_done")
        pick_out = sem("pick_out")
        late_onehot = sem("late_onehot")
        late_out = sem("late_out")
        dense_ready = sem("dense_ready")
        dense_out = sem("dense_out")
        tr_ready = sem("tr_ready")
        tr_out_dve = sem("tr_out_dve")
        tr_out_act = sem("tr_out_act")
        gram_ready = sem("gram_ready")
        gram_out_dve = sem("gram_out_dve")
        gram_out_act = sem("gram_out_act")
        pairs_ready = sem("pairs_ready")
        packed_dve = sem("packed_dve")
        packed_act = sem("packed_act")
        back_ready = sem("back_ready")
        back_out_dve = sem("back_out_dve")
        back_out_act = sem("back_out_act")
        h1_ready = sem("h1_ready")
        h1_out_dve = sem("h1_out_dve")
        h1_out_act = sem("h1_out_act")
        h2_ready = sem("h2_ready")
        h2_out_dve = sem("h2_out_dve")
        h2_out_act = sem("h2_out_act")
        y_ready = sem("y_ready")
        y_out = sem("y_out")
        stored = sem("stored")

        block = ctx.enter_context(nc.Block())

        def rows_by_dma(t, n):
            return [s for s in BANK_SLOTS[n] if not (t == TILES - 1 and SLOT_FIELD[s] == LATE)]

        def gram_block(s, q):
            return gram_sb[PAD * q:PAD * q + NJ, :, s * SET_G:(s + 1) * SET_G]

        def gram_block_ps(s, q):
            v = gram_ps[s % GRAM_BANKS][PAD * q:PAD * q + NJ, 0:SET_G * Q * NJ].rearrange("i (g n) -> i g n", g=SET_G)
            return v[:, :, q * NJ:(q + 1) * NJ].rearrange("i g j -> i j g")

        def group_order(bank, w):
            return bank[:, 0:w, :].rearrange("d s (q g) -> d g q s", q=Q)

        def tile_slots(t, n):
            slots = BANK_SLOTS[n]
            return xt[:, t, :, slots[0]:slots[-1] + 1].rearrange("d (g q) s -> d g q s", q=Q)

        def rect(r):
            j0, nj = RECTS[r]
            ni = j0 + nj - 1
            to = packed[:, rect_at(r):rect_at(r) + nj * ni].rearrange("p (j i) -> p j i", j=nj)
            return to, pairs[:, j0 - 1:j0 - 1 + nj, 0:ni]

        @block.sync
        def _(sp):
            sp.dma_start(ids_sb[:], ids.rearrange("(p t) f -> p t f", t=TILES)).then_inc(ids_in, 16)
            for o, f in enumerate(ONEHOT + [LATE]):
                if o >= TABLES:
                    sp.wait_ge(low_ready, o - TABLES + 1)
                sp.dma_start(table[0:OH_K, o % TABLES], tables[f].rearrange("(p c) d -> p c d", c=OH_CHUNKS)
                             ).then_inc(table_in[o % TABLES], 16)
                if o == TABLES - 1:
                    sp.dma_start(dense_sb[:], dense.rearrange("(p t) d -> p t d", t=TILES)).then_inc(dense_in, 16)
                    sp.dma_start(w1p_sb[:], w1_pairs).then_inc(weights_in, 16)
                    sp.dma_start(w1d_sb[:], w1_dense).then_inc(weights_in, 16)
                    sp.dma_start(w2_sb[:], w2.rearrange("(c k) n -> k c n", k=P)).then_inc(weights_in, 16)
                    sp.dma_start(w3_sb[:], w3).then_inc(weights_in, 16)
                    sp.dma_start(b1_sb[:], b1).then_inc(weights_in, 16)
                    sp.dma_start(b2_sb[:], b2).then_inc(weights_in, 16)
            sp.wait_ge(y_out, TILES)
            sp.dma_start(out.rearrange("(p t) o -> p (t o)", t=TILES), y_sb[:]).then_inc(stored, 16)
            sp.wait_ge(stored, 16)

        @block.gpsimd
        def _(pool):
            pool.memset(ident[:], 0.0).then_inc(ident_zero, 1)
            pool.iota(field_of[:], pattern=[[OH_CHUNKS, NO + 1]], base=0, channel_multiplier=0).then_inc(row_ready, 1)
            pool.iota(row_of[:], pattern=[[1, OH_CHUNKS]], base=0, channel_multiplier=OH_CHUNKS).then_inc(row_ready, 1)
            pool.wait_ge(ident_zero, 1)
            pool.affine_select(out=ident[:], in_=ident[:], compare_op=ALU.not_equal, fill=1.0, base=0,
                               pattern=[[-1, P]], channel_multiplier=1).then_inc(ident_ready, 1)
            pool.wait_ge(ids_in, 16)
            for t in range(TILES):
                for n in range(NT):
                    for s in rows_by_dma(t, n):
                        f = SLOT_FIELD[s]
                        pool.indirect_dma_start(rows[:, t, s - 1, :], None, tables[f],
                                                bass.IndirectOffsetOnAxis(ids_sb[:, t, f:f + 1], 0)
                                                ).then_inc(gathered[t][n], 16)


        @block.scalar
        def _(act):
            act.dma_start(field_ids[:], ids_by_field).then_inc(field_ids_in, 16)

            def picked(o):
                act.wait_ge(pick_done, o + 1)
                act.activation(xt[:, :, :, NG + 1 + o], pick_ps[o % 2][:].rearrange("d (t p) -> d t p", t=TILES),
                               ACT.Copy).then_inc(pick_out, 1)

            def transposed(t, banks):
                for n in banks:
                    if n % 2 == 1:
                        act.wait_ge(tr_ready, t * NT + (n + 1))
                        act.activation(tile_slots(t, n), group_order(tr_ps[1], len(BANK_SLOTS[n])), ACT.Copy
                                       ).then_inc(tr_out_act, 1)

            def gram(t, sets=range(SETS)):
                for s in sets:
                    act.wait_ge(gram_ready, t * SETS + (s + 1))
                    for q in (0, 1):
                        last = act.activation(gram_block(s, q), gram_block_ps(s, q), ACT.Copy)
                    last.then_inc(gram_out_act, 1)

            def split_late(half):
                if half == 0:
                    act.wait_ge(pick_done, NO - 1)
                    act.wait_ge(table_in[NO % TABLES], 16 * (NO // TABLES + 1))
                c = slice(half * (OH_CHUNKS // 2), (half + 1) * (OH_CHUNKS // 2))
                act.activation(high[0:OH_K, NO % 2, c], table[0:OH_K, NO % TABLES, c], ACT.Copy).then_inc(high_ready, 1)

            def back(n):
                act.wait_ge(back_ready, n)
                act.activation(pairs_t[:, 0:NC - 1, :].rearrange("k c p -> k (c p)"), gram_ps[0][:, 0:(NC - 1) * P],
                               ACT.Copy).then_inc(back_out_act, 1)

            def first_layer(n):
                act.wait_ge(h1_ready, n * (N1 // P))
                for m in (0, 1):
                    act.activation(h1[:, m, :], h1_ps[m], ACT.Relu, bias=b1_sb[:, m:m + 1]).then_inc(h1_out_act, 1)

            def second_layer(n):
                act.wait_ge(h2_ready, n)
                for m in (0, 1):
                    last = act.activation(h2[:, m, :], h2_ps[m], ACT.Relu, bias=b2_sb[:, m:m + 1])
                last.then_inc(h2_out_act, 1)

            def third_layer(n):
                act.wait_ge(y_ready, n)
                act.activation(y_sb[:, bass.ds(n - 1, 1)], y_ps, ACT.Copy).then_inc(y_out, 1)

            def pack(n):
                act.wait_ge(pairs_ready, 2 * n)
                for r in ACT_RECTS_EARLY:
                    act.activation(*rect(r), ACT.Copy)
                act.wait_ge(pairs_ready, 2 * n + 1)
                for r in ACT_RECTS_LATE:
                    last = act.activation(*rect(r), ACT.Copy)
                last.then_inc(packed_act, 1)

            def step(t, third):
                if third:
                    transposed(t, (0, 1))
                pack(t)
                if third:
                    second_layer(t - 1)
                back(t)
                transposed(t, (2, 3))
                if not third:
                    act.wait_ge(pick_done, NO + 1)
                    act.activation(rows[:, TILES - 1, SLOT_FIELD.index(LATE) - 1, :], late_ps, ACT.Copy
                                   ).then_inc(late_out, 1)
                if third:
                    third_layer(t - 1)
                transposed(t, range(4, NT))
                first_layer(t)
                gram(t)

            def act_part(c):
                return (0, SHARED_COLS) if c == SHARED else ((c - SHARED) * B - SHARED_COLS, 0)

            def onehots(o):
                act.wait_ge(ids_spread, o + 1)
                if o:
                    act.wait_ge(onehot_act, o)
                for c in range(SHARED, OH_CHUNKS):
                    at, cols = act_part(c)
                    last = act.activation(distance[0:OH_K, at:at + B - cols], ids_ps_act[o % 2][0:OH_K, cols:], ACT.Abs,
                                          bias=row_neg[0:OH_K, c:c + 1])
                last.then_inc(distance_ready, 1)
                if o >= 2:
                    act.wait_ge(pick_done, o - 1)
                act.wait_ge(table_in[o % TABLES], 16 * (o // TABLES + 1))
                act.activation(high[0:OH_K, o % 2], table[0:OH_K, o % TABLES], ACT.Copy).then_inc(high_ready, 1)
                act.wait_ge(distance_ready, o + 1)
                act.activation(onehot[0:OH_K, o % 2].rearrange("k c b -> k (c b)")[:, OH_CHUNKS * B - ACT_COLS:],
                               distance[0:OH_K], ACT.Relu, scale=-1.0, bias=1.0).then_inc(onehot_act, 1)

            act.wait_ge(row_f_ready, 1)
            act.activation(row_neg[:], row_f[:], ACT.Copy, scale=-1.0).then_inc(row_neg_ready, 1)
            act.wait_ge(zeros_ready, 1)
            act.activation(xt[:, :, :, N_SLOTS:PAD].rearrange("d t p s -> d (t p) s"),
                           zeros[:].rearrange("d (b s) -> d b s", s=1).to_broadcast([P, B, PAD - N_SLOTS]), ACT.Copy
                           ).then_inc(pad_zero, 1)
            act.wait_ge(row_neg_ready, 1)
            for o in range(NO):
                if o == NO - 1:
                    transposed(0, (0, 1))
                onehots(o)
                if o >= 1:
                    picked(o - 1)
                if o == 2:
                    act.wait_ge(dense_ready, 1)
                    act.activation(xt[:, :, :, 0].rearrange("d t (g q) -> d t g q", q=Q),
                                   tr_ps[0][:, :, :].rearrange("d t (q g) -> d t g q", q=Q), ACT.Copy)
                    act.activation(dense_t[:], tr_ps[0][:, :, :], ACT.Copy).then_inc(dense_out, 1)
            transposed(0, range(2, NT))
            picked(NO - 1)
            transposed(1, (0, 1))
            act.wait_ge(pairs_ready, 1)
            for s in range(SETS):
                gram(0, (s,))
                if s in (0, 1):
                    split_late(s)
            act.wait_ge(weights_in, WEIGHTS)
            step(1, False)
            with act.Fori(2, TILES) as t:
                step(t, True)
            pack(TILES)
            second_layer(TILES - 1)
            back(TILES)
            third_layer(TILES - 1)
            for k, m in enumerate((0, 1)):
                act.wait_ge(h1_ready, (TILES - 1) * (N1 // P) + 2 * k + 1)
                act.activation(h1[:, m, :], h1_ps_last[m], ACT.Relu, bias=b1_sb[:, m:m + 1]).then_inc(h1_out_act, 1)
            act.wait_ge(h2_ready, TILES)
            act.activation(h2[:, 0, :], h2_ps_last[0], ACT.Relu, bias=b2_sb[:, 0:1]).then_inc(h2_out_act, 1)
            third_layer(TILES)

        @block.vector
        def _(dve):
            dve.memset(zeros[:], 0.0).then_inc(zeros_ready, 1)
            dve.wait_ge(row_ready, 2)
            dve.tensor_copy(row_f[:], row_of[:]).then_inc(row_f_ready, 1)
            dve.wait_ge(row_f_ready, 1)
            dve.tensor_scalar(select[:], field_of[:].rearrange("k (o p) -> k o p", p=1
                                                               ).to_broadcast([NO + 1, NO + 1, OH_K]),
                              row_f[0:NO + 1, 0:1], None, ALU.is_equal).then_inc(select_ready, 1)
            dve.wait_ge(field_ids_in, 16)
            dve.tensor_copy(field_ids16[:], field_ids[:]).then_inc(ids16_ready, 1)

            def transposed(t, banks):
                for n in banks:
                    if n % 2 == 0:
                        dve.wait_ge(tr_ready, t * NT + (n + 1))
                        dve.tensor_copy(tile_slots(t, n), group_order(tr_ps[0], len(BANK_SLOTS[n]))
                                        ).then_inc(tr_out_dve, 1)

            for o in range(NO):
                b = o % 2
                if o == NO - 1:
                    transposed(0, (0, 1))
                dve.wait_ge(ids_spread, o + 1)
                if o >= 2:
                    dve.wait_ge(pick_done, o - 1)
                for cs in DVE_CHUNKS:
                    shape = [OH_K, len(cs), B]
                    dve.tensor_tensor(onehot[0:OH_K, b, cs[0]:cs[-1] + 1],
                                      ids_ps_dve[b][0:OH_K].rearrange("k (c b) -> k c b", c=1).to_broadcast(shape),
                                      row_f[0:OH_K, cs[0]:cs[-1] + 1].rearrange("k (c b) -> k c b", b=1
                                                                                ).to_broadcast(shape),
                                      ALU.is_equal).then_inc(onehot_dve, 1)
                dve.tensor_scalar(onehot[0:OH_K, b, SHARED, 0:SHARED_COLS], ids_ps_dve[b][0:OH_K, 0:SHARED_COLS],
                                  row_f[0:OH_K, SHARED:SHARED + 1], None, ALU.is_equal).then_inc(onehot_dve, 1)
                dve.wait_ge(high_ready, o + 1)
                dve.tensor_tensor(low[0:OH_K, b], table[0:OH_K, o % TABLES], high[0:OH_K, b].bitcast(F32),
                                  ALU.subtract).then_inc(low_ready, 1)

            def gram(t, sets=range(SETS)):
                for s in sets:
                    dve.wait_ge(gram_ready, t * SETS + (s + 1))
                    for q in (2, 3):
                        last = dve.tensor_copy(gram_block(s, q), gram_block_ps(s, q))
                    last.then_inc(gram_out_dve, 1)

            def onehot_late(half):
                c0, n = half * (OH_CHUNKS // 2), OH_CHUNKS // 2
                if half == 0:
                    dve.wait_ge(ids_spread, NO + 1)
                    dve.wait_ge(pick_done, NO - 1)
                dve.tensor_tensor(onehot[0:OH_K, NO % 2, c0:c0 + n, 0:P],
                                  late_ids_ps[0:OH_K].rearrange("k (c b) -> k c b", c=1).to_broadcast([OH_K, n, P]),
                                  row_f[0:OH_K, c0:c0 + n].rearrange("k (c b) -> k c b", b=1
                                                                     ).to_broadcast([OH_K, n, P]),
                                  ALU.is_equal).then_inc(late_onehot, 1)

            def rest_late(half):
                dve.wait_ge(high_ready, NO + half + 1)
                c = slice(half * (OH_CHUNKS // 2), (half + 1) * (OH_CHUNKS // 2))
                dve.tensor_tensor(low[0:OH_K, NO % 2, c], table[0:OH_K, NO % TABLES, c],
                                  high[0:OH_K, NO % 2, c].bitcast(F32), ALU.subtract).then_inc(low_ready, 1)

            def squares(n):
                dve.wait_ge(gram_out_act, n * SETS)
                dve.wait_ge(gram_out_dve, n * SETS)
                for j in (slice(EARLY_J, NJ), slice(0, EARLY_J)):
                    dve.transpose(pairs[:, j].rearrange("p j i -> p (j i)"), gram_sb[:, j].rearrange("p j g -> p (j g)")
                                  ).then_inc(pairs_ready, 1)

            def pack(n):
                dve.wait_ge(pairs_ready, 2 * n + 1)
                for r in range(len(RECTS)):
                    if r not in ACT_RECTS_EARLY + ACT_RECTS_LATE:
                        last = dve.tensor_copy(*rect(r))
                last.then_inc(packed_dve, 1)

            def back(n):
                dve.wait_ge(back_ready, n)
                dve.tensor_copy(pairs_t[:, NC - 1, :], gram_ps[1][:, 0:P]).then_inc(back_out_dve, 1)

            def first_layer(n):
                dve.wait_ge(h1_ready, n * (N1 // P))
                for m in (2, 3):
                    dve.tensor_scalar(h1[:, m, :], h1_ps[m], b1_sb[:, m:m + 1], 0.0, ALU.add, ALU.max
                                      ).then_inc(h1_out_dve, 1)

            transposed(0, range(2, NT))
            dve.memset(packed[:, N_PACKED:], 0.0)
            dve.memset(gram_sb[:], 0.0).then_inc(pairs_ready, 1)
            transposed(1, (0, 1))
            dve.wait_ge(pairs_ready, 1)
            for s in range(SETS):
                gram(0, (s,))
                if s in (1, 2):
                    onehot_late(s - 1)
                elif s in (3, 4):
                    rest_late(s - 3)
            dve.wait_ge(weights_in, WEIGHTS)
            squares(1)
            pack(1)
            back(1)
            transposed(1, range(2, NT))
            first_layer(1)
            gram(1)
            with dve.Fori(2, TILES) as t:
                squares(t)
                pack(t)
                transposed(t, (0, 1))
                back(t)
                transposed(t, range(2, NT))
                first_layer(t)
                gram(t)
            squares(TILES)
            pack(TILES)
            back(TILES)
            for k, m in enumerate((2, 3)):
                dve.wait_ge(h1_ready, (TILES - 1) * (N1 // P) + 2 * k + 2)
                dve.tensor_scalar(h1[:, m, :], h1_ps_last[m], b1_sb[:, m:m + 1], 0.0, ALU.add, ALU.max
                                  ).then_inc(h1_out_dve, 1)
            dve.wait_ge(h2_ready, TILES + 1)
            dve.tensor_scalar(h2[:, 1, :], h2_ps_last[1], b2_sb[:, 1:2], 0.0, ALU.add, ALU.max
                              ).then_inc(h2_out_dve, 1)

        @block.tensor
        def _(pe):

            def spread(o):
                for ps in (ids_ps_dve[o % 2], ids_ps_act[o % 2]):
                    last = pe.matmul(ps[0:OH_K], select[:, o, :], field_ids16[:], start=True, stop=True)
                last.then_inc(ids_spread, 1)

            def pick(o, part):
                b = o % 2
                if part == 0:
                    if o >= 2:
                        pe.wait_ge(pick_out, o - 1)
                    pe.wait_ge(high_ready, o + 1)
                    weights = high[0:OH_K, b]
                else:
                    pe.wait_ge(low_ready, o + 1)
                    weights = low[0:OH_K, b]
                for c in range(OH_CHUNKS):
                    if part == 0:
                        if c < SHARED:
                            made = [c in cs for cs in DVE_CHUNKS].index(True) + 1
                        else:
                            made = len(DVE_CHUNKS) + 1
                            pe.wait_ge(onehot_act, o + 1)
                        pe.wait_ge(onehot_dve, (len(DVE_CHUNKS) + 1) * o + made)
                    last = pe.matmul(pick_ps[b][:], weights[:, c, :], onehot[0:OH_K, b, c, :],
                                     start=(c == 0 and part == 0), stop=(c == OH_CHUNKS - 1 and part == 1))
                if part == 1:
                    last.then_inc(pick_done, 1)

            def pick_late(part):
                if part == 0:
                    pe.wait_ge(late_onehot, 2)
                    pe.wait_ge(high_ready, NO + 2)
                else:
                    pe.wait_ge(low_ready, NO + 2)
                values = (high, low)[part]
                for c in range(OH_CHUNKS):
                    last = pe.matmul(late_ps, onehot[0:OH_K, NO % 2, c, 0:P], values[0:OH_K, NO % 2, c, :],
                                     start=(c == 0 and part == 0), stop=(c == OH_CHUNKS - 1 and part == 1))
                if part == 1:
                    last.then_inc(pick_done, 1)

            def transposes(t, banks):
                for n in banks:
                    pe.wait_ge(gathered[t][n], 16 * len(rows_by_dma(t, n)))
                    if t == TILES - 1 and SLOT_FIELD.index(LATE) in BANK_SLOTS[n]:
                        pe.wait_ge(late_out, 1)
                    out_of = (tr_out_dve, tr_out_act)[n % 2]
                    before = t * TR_OUT[n % 2] + n // 2
                    if before:
                        pe.wait_ge(out_of, before)
                    elif n == 0:
                        pe.wait_ge(dense_out, 1)
                    for s in BANK_SLOTS[n]:
                        last = pe.transpose(tr_ps[n % 2][:, s - BANK_SLOTS[n][0], :], rows[:, t, s - 1, :], ident[:])
                    last.then_inc(tr_ready, 1)

            def gram(t):
                pe.wait_ge(tr_out_dve, (t + 1) * TR_OUT[0])
                pe.wait_ge(tr_out_act, (t + 1) * TR_OUT[1])
                for s in range(SETS):
                    if s >= GRAM_BANKS:
                        pe.wait_ge(gram_out_act, t * SETS + s - GRAM_BANKS + 1)
                        pe.wait_ge(gram_out_dve, t * SETS + s - GRAM_BANKS + 1)
                    for k in range(SET_G):
                        g = s * SET_G + k
                        group = xt[:, t, Q * g:Q * (g + 1), :]
                        weights = group.rearrange("d q i -> d (q i)")[:, 0:(Q - 1) * PAD + NJ]
                        last = pe.matmul(gram_ps[s % GRAM_BANKS][0:(Q - 1) * PAD + NJ, k * Q * NJ:(k + 1) * Q * NJ],
                                         weights, group[:, :, 1:N_SLOTS], start=True, stop=True)
                    last.then_inc(gram_ready, 1)

            def dense_part(t, parts=range(N1 // P)):
                if t:
                    pe.wait_ge(h1_out_act, 2 * t)
                    pe.wait_ge(h1_out_dve, 2 * t)
                ps = h1_banks(t)
                for m in parts:
                    pe.matmul(ps[m], w1d_sb[:, m * P:(m + 1) * P], dense_t[:, t, :],
                              start=(m % 2 == 0 or t == TILES - 1), stop=False, skip_group_check=True)

            def back(t):
                pe.wait_ge(packed_act, t + 1)
                pe.wait_ge(packed_dve, t + 1)
                for c in range(NC):
                    last = pe.transpose(gram_ps[0][:, c * P:(c + 1) * P] if c < NC - 1 else gram_ps[1][:, 0:P],
                                        packed[:, c * P:(c + 1) * P], ident[:])
                last.then_inc(back_ready, 1)

            def h1_banks(t):
                return h1_ps_last if t == TILES - 1 else h1_ps

            def first_layer(t, parts):
                pe.wait_ge(back_out_act, t + 1)
                pe.wait_ge(back_out_dve, t + 1)
                for m in parts:
                    for c in range(NC):
                        last = pe.matmul(h1_banks(t)[m], w1p_sb[:, c, m * P:(m + 1) * P], pairs_t[:, c, :],
                                         start=False, stop=(c == NC - 1), skip_group_check=True)
                    last.then_inc(h1_ready, 1)

            def second_layer(t):
                if t:
                    pe.wait_ge(y_out, t)
                pe.wait_ge(h1_out_act, 2 * t + 2)
                pe.wait_ge(h1_out_dve, 2 * t + 2)
                for m in range(N2 // P):
                    for c in range(N1 // P):
                        last = pe.matmul(h2_ps[m], w2_sb[:, c, m * P:(m + 1) * P], h1[:, c, :],
                                         start=(c == 0), stop=(c == N1 // P - 1))
                last.then_inc(h2_ready, 1)

            def second_layer_last(t):
                pe.wait_ge(h1_out_act, 2 * t + 1)
                pe.wait_ge(h1_out_dve, 2 * t + 1)
                for c, m in ((0, 0), (0, 1), (2, 0), (2, 1), (1, 0), (3, 0), (1, 1), (3, 1)):
                    if c % 2 and m == 0:
                        pe.wait_ge((h1_out_act, h1_out_dve)[c // 2], 2 * t + 2)
                    last = pe.matmul(h2_ps_last[m], w2_sb[:, c, m * P:(m + 1) * P], h1[:, c, :],
                                     start=(c == 0), stop=(c == 3))
                    if c == 3:
                        last.then_inc(h2_ready, 1)

            def third_layer(t):
                pe.wait_ge(h2_out_act, t + 1)
                if t:
                    pe.wait_ge(y_out, t)
                for c in range(N2 // P):
                    if t == TILES - 1 and c == 1:
                        pe.wait_ge(h2_out_dve, 1)
                    last = pe.matmul(y_ps, h2[:, c, :], w3_sb[:, c:c + 1], start=(c == 0),
                                     stop=(c == N2 // P - 1))
                last.then_inc(y_ready, 1)

            pe.wait_ge(zeros_ready, 1)
            for _ in range(WARM_UP[0]):
                pe.matmul(tr_ps[1][:].rearrange("p s n -> p (s n)"), zeros[:, 0:P], zeros[:], start=True, stop=True)
            pe.wait_ge(select_ready, 1)
            pe.wait_ge(ids16_ready, 1)
            spread(0)
            for _ in range(WARM_UP[1]):
                pe.matmul(tr_ps[1][:].rearrange("p s n -> p (s n)"), zeros[:, 0:P], zeros[:], start=True, stop=True)
            spread(1)
            for o in range(NO - 1):
                pick(o, 0)
                if o + 2 < NO:
                    spread(o + 2)
                pick(o, 1)
                if o == NO - 3:
                    transposes(0, (0, 1))
                if o == NO - 2:
                    transposes(0, (2, 3))
                if o == 1:
                    pe.wait_ge(ident_ready, 1)
                    pe.wait_ge(dense_in, 16)
                    for t in range(TILES):
                        last = pe.transpose(tr_ps[0][:, t, :], dense_sb[:, t, :], ident[:])
                    last.then_inc(dense_ready, 1)
            pick(NO - 1, 0)
            transposes(0, range(4, NT))
            pick(NO - 1, 1)
            transposes(1, (0, 1))
            pe.matmul(late_ids_ps[0:OH_K], select[:, NO, :], field_ids16[:, (TILES - 1) * P:], start=True, stop=True
                      ).then_inc(ids_spread, 1)
            pe.wait_ge(pad_zero, 1)
            pe.wait_ge(pick_out, NO)
            gram(0)
            for t in range(1, TILES):
                if t == 1:
                    pe.wait_ge(weights_in, WEIGHTS)
                    dense_part(0)
                    transposes(1, (2, 3))
                    pick_late(0)
                    back(0)
                    pick_late(1)
                else:
                    transposes(t, (0, 1))
                    dense_part(t - 1)
                    if t == 2:
                        pe.wait_ge(late_out, 1)
                    second_layer(t - 2)
                    back(t - 1)
                    transposes(t, (2, 3))
                    third_layer(t - 2)
                first_layer(t - 1, (0, 2))
                if t < TILES - 1:
                    transposes(t, range(4, NT))
                first_layer(t - 1, (1,))
                if t == TILES - 1:
                    transposes(t, range(4, NT))
                first_layer(t - 1, (3,))
                gram(t)
            second_layer(TILES - 2)
            dense_part(TILES - 1, (0, 2))
            back(TILES - 1)
            dense_part(TILES - 1, (1, 3))
            third_layer(TILES - 2)
            first_layer(TILES - 1, (0, 2, 1, 3))
            second_layer_last(TILES - 1)
            third_layer(TILES - 1)


def pair_row(i, j):
    a, b = sorted((SLOT_FIELD[i], SLOT_FIELD[j]))
    return a * (2 * N_SLOTS - a - 1) // 2 + (b - a - 1)


def kernel(**inputs):
    import concourse.bacc as bacc
    from concourse.bass_utils import run_bass_kernel_spmd as run

    a = {k: np.ascontiguousarray(v) for k, v in inputs.items()}
    w1 = a["W_top1"]
    n_pairs = N_SLOTS * (N_SLOTS - 1) // 2
    w1_pairs = np.zeros((P, NC, N1), w1.dtype)
    for r, (j0, nj) in enumerate(RECTS):
        for j in range(j0, j0 + nj):
            for i in range(j):
                c, k = divmod(rect_at(r) + (j - j0) * (j0 + nj - 1) + i, P)
                w1_pairs[k, c] = w1[pair_row(i, j)]
    laid = {
        "dense": a["r_dense_x"],
        "ids": a["ids"],
        "ids_by_field": np.concatenate([
            a["ids"].reshape(Q, G, TILES, N_FIELDS).transpose(3, 2, 1, 0).reshape(N_FIELDS, B)[ONEHOT],
            a["ids"].reshape(P, TILES, N_FIELDS).transpose(2, 1, 0).reshape(N_FIELDS, B)[[LATE]]]),
        "w1_pairs": w1_pairs,
        "w1_dense": np.ascontiguousarray(w1[n_pairs:]),
        "b1": np.ascontiguousarray(a["b_top1"].reshape(N1 // P, P).T),
        "w2": a["W_top2"],
        "b2": np.ascontiguousarray(a["b_top2"].reshape(N2 // P, P).T),
        "w3": np.ascontiguousarray(a["W_top3"].reshape(N2 // P, P).T),
    }
    for f in range(N_FIELDS):
        laid[f"table{f}"] = a[f"tbl_{f}"]

    nc = bacc.Bacc("TRN2", target_bir_lowering=False, num_devices=1)
    ap = {k: nc.dram_tensor(k, v.shape, mybir.dt.from_np(v.dtype), kind="ExternalInput").ap() for k, v in laid.items()}
    out = nc.dram_tensor("y", (B, 1), F32, kind="ExternalOutput").ap()
    tower(nc, ap["dense"], ap["ids"], ap["ids_by_field"], [ap[f"table{f}"] for f in range(N_FIELDS)],
          ap["w1_pairs"], ap["w1_dense"], ap["b1"], ap["w2"], ap["b2"], ap["w3"], out)
    return run(nc, [laid], core_ids=[0]).results[0]["y"]
```
